# Optimizing a Trainium2 kernel written in Bass

```python
import numpy as np
import jax
import jax.numpy as jnp

def _softmax(x, axis=-1):
    return jax.nn.softmax(x, axis=axis)

def _gelu(x):
    return jax.nn.gelu(x, approximate=True)

def _silu(x):
    return jax.nn.silu(x)

def _sigmoid(x):
    return jax.nn.sigmoid(x)

def _layernorm(x, axis=-1, eps=1e-05):
    m = jnp.mean(x, axis=axis, keepdims=True)
    v = jnp.var(x, axis=axis, keepdims=True)
    return (x - m) / jnp.sqrt(v + eps)

def _scatter_add(tgt, idx, src, axis=0):
    return tgt.at[idx].add(src)

def _segment_sum(src, seg, n):
    return jax.ops.segment_sum(src, seg, n)
kernel_name = 'mk_cond_resid_d2_seqx_r4_6943b0'

def setup_inputs(seed: int=0):
    np.random.seed(seed)
    _w = jnp.asarray

    def _rec_inputs():
        import jax
        import jax.numpy as jnp
        _rk = jax.random.key(seed)
        x = -7.109e-05 + 0.9999 * jax.random.normal(jax.random.fold_in(_rk, 1), (128, 64, 1024), jnp.float32)
        _lenS = 64 - jax.random.randint(jax.random.fold_in(_rk, 7), (128,), 0, max(1, 64 // 4) + 1, jnp.int32)
        _lenS2 = 64 - jax.random.randint(jax.random.fold_in(_rk, 8), (128,), 0, max(1, 64 // 4) + 1, jnp.int32)
        itok_B_0_15 = jax.random.randint(jax.random.fold_in(_rk, 11), (128,), 0, 16, jnp.int32)
        itok_B_4_50 = jax.random.randint(jax.random.fold_in(_rk, 12), (128,), 4, 51, jnp.int32)
        return (x, itok_B_0_15, itok_B_4_50)
    x, itok_B_0_15, itok_B_4_50 = _rec_inputs()

    def _L0_cond_setup():
        import jax, jax.numpy as jnp
        import numpy as np
        NUM_CONDITIONS = 16
        IN_CH = 64
        OUT_CH = 64
        B = 64
        T = 1024
        key = jax.random.key(seed)
        k_x, k_w, k_c = jax.random.split(key, 3)
        x = jax.random.normal(k_x, (B, IN_CH, T), dtype=jnp.float32)
        bound = float(np.sqrt(6.0 / IN_CH))
        weights = jax.random.uniform(k_w, (NUM_CONDITIONS, IN_CH, OUT_CH), dtype=jnp.float32, minval=-bound, maxval=bound)
        condition = jax.random.randint(k_c, (B,), 0, NUM_CONDITIONS, dtype=jnp.int64)
        return {'x': x, 'weights': weights, 'condition': condition}
    _L0_cond_all = _L0_cond_setup()
    _L0_cond_in = {k: v for k, v in _L0_cond_all.items() if k in ('weights',)}
    del _L0_cond_all

    def _L1_cond_setup():
        import jax, jax.numpy as jnp
        import numpy as np
        RANK = 16
        ALPHA = 16.0
        SCALING = ALPHA / RANK
        key = jax.random.key(seed)
        k1, k2, k3, k4 = jax.random.split(key, 4)
        batch, n_tok, d_in, d_out, n_adapters, rank = (8, 512, 1024, 1024, 64, RANK)
        x = jax.random.normal(k1, (batch, n_tok, d_in), dtype=jnp.float32)
        A = jax.random.normal(k2, (n_adapters, d_out, rank), dtype=jnp.float32) * 0.02
        B = jax.random.normal(k3, (n_adapters, rank, d_in), dtype=jnp.float32)
        adapter_ids = jax.random.randint(k4, (batch,), 0, n_adapters, dtype=jnp.int32)
        return {'x': x, 'A': A, 'B': B, 'adapter_ids': adapter_ids}
    _L1_cond_all = _L1_cond_setup()
    _L1_cond_in = {k: v for k, v in _L1_cond_all.items() if k in ('A', 'B')}
    del _L1_cond_all
    return {'x': x, 'itok_B_0_15': itok_B_0_15, 'itok_B_4_50': itok_B_4_50, 'L0_cond_weights': _L0_cond_in['weights'], 'L1_cond_A': _L1_cond_in['A'], 'L1_cond_B': _L1_cond_in['B']}

def reference(x, itok_B_0_15, itok_B_4_50, L0_cond_weights, L1_cond_A, L1_cond_B):
    import jax
    import jax.numpy as jnp

    def _L0_cond_ref(x, weights, condition):
        import jax, jax.numpy as jnp
        import numpy as np
        NUM_CONDITIONS = 16
        IN_CH = 64
        OUT_CH = 64
        B = 64
        T = 1024
        W = weights[condition]
        return jnp.einsum('bct,bcd->bdt', x, W)

    def _L1_cond_ref(x, A, B, adapter_ids):
        import jax, jax.numpy as jnp
        import numpy as np
        RANK = 16
        ALPHA = 16.0
        SCALING = ALPHA / RANK
        B_req = B[adapter_ids]
        A_req = A[adapter_ids]
        Bx = jnp.einsum('bni,bri->bnr', x, B_req)
        out = jnp.einsum('bnr,bor->bno', Bx, A_req)
        return out * SCALING
    x = x + _L0_cond_ref(x, L0_cond_weights, itok_B_0_15)
    x = x + _L1_cond_ref(x, L1_cond_A, L1_cond_B, itok_B_4_50)
    return x

_drawn_inputs = setup_inputs


def setup_inputs(seed=0):
    import zlib

    import numpy as np

    out = dict(_drawn_inputs(seed))
    spreads = {}
    factors = {}
    for name, (base, spread) in spreads.items():
        noise = np.random.default_rng([zlib.crc32(name.encode()), seed]).standard_normal(out[name].shape)
        drawn = base * np.exp(spread * noise) if base else spread * noise
        out[name] = jnp.asarray(drawn.astype(out[name].dtype))
    for name, factor in factors.items():
        out[name] = (out[name] * factor).astype(out[name].dtype)
    return out
```

```python
from contextlib import ExitStack

import concourse.bass as bass
from concourse import mybir

F32 = mybir.dt.float32
I32 = mybir.dt.int32
ALU = mybir.AluOpType
AX_X = mybir.AxisListType.X

P = 128
UNROLL = 4
A_RAWS = 4
TABLE_UNROLL = 4


def wait(engine, semaphore, value):
    if not isinstance(value, int) or value > 0:
        engine.wait_ge(semaphore, value)


def cond_lora_kernel(nc, x, cond_ids, adapter_ids, cond_w, lora_a, lora_b, out):
    BATCH, C, T = x.shape
    CONDS = cond_w.shape[0]
    ADAPTERS, _, R = lora_a.shape
    PAIRS = BATCH // 2
    CHUNKS = T // P
    BANK = 512
    HALVES = T // BANK
    PER_SLAB = C // R
    SLABS = ADAPTERS // PER_SLAB
    PER_GROUP = P // R
    GROUPS = ADAPTERS // PER_GROUP
    QUADS = 4
    assert 2 * C == P and 2 * R * QUADS == P and CHUNKS == 2 * QUADS and HALVES == 2
    assert PAIRS % UNROLL == 0 and GROUPS % TABLE_UNROLL == 0 and CONDS * C == T

    a_loads = lora_a.rearrange("(g q e) (w s) r -> g q w e (s r)", q=QUADS, e=2, s=32)
    b_loads = lora_b.rearrange("(l g a) r t -> l (a r) g t", g=2, a=PER_GROUP)
    x_pairs = x.rearrange("(n a) c t -> n a c t", a=2)
    out_pairs = out.rearrange("(n a) c t -> n (a c) t", a=2)

    with ExitStack() as ctx:

        def sb(name, shape, dtype=F32):
            return ctx.enter_context(nc.sbuf_tensor(name, shape, dtype))

        def sem(name):
            return ctx.enter_context(nc.semaphore(name))

        at_table = sb("at_table", [P, SLABS, T])
        bt_table = sb("bt_table", [P, CHUNKS, ADAPTERS, R])
        m_table = sb("m_table", [P, CONDS, C])
        ident = sb("ident", [P, P])
        ident2 = sb("ident2", [P, C])
        ids = sb("ids", [1, 2, BATCH], I32)
        offsets = sb("offsets", [1, 4, BATCH], I32)
        in_slab_row = sb("in_slab_row", [1, BATCH], I32)
        slab_row = sb("slab_row", [1, BATCH], I32)
        ids_all = sb("ids_all", [P, BATCH], I32)
        in_slab = sb("in_slab", [P, BATCH], I32)
        slab_mask = sb("slab_mask", [P, PAIRS, PER_SLAB])

        a_raw = sb("a_raw", [P, A_RAWS, 2, 32 * R])
        b_raw = sb("b_raw", [P, 2, 2, T])

        moving = sb("moving", [P, UNROLL, 2, T])
        weights = sb("weights", [P, UNROLL, 2, C])
        b_pair = sb("b_pair", [P, UNROLL, CHUNKS, 2, R])
        x_t = sb("x_t", [P, 2, CHUNKS, P])
        result = sb("result", [P, UNROLL, T])
        bx_parts = sb("bx_parts", [P, P])
        bx = sb("bx", [P, R])
        bx_spread = sb("bx_spread", [P, PER_SLAB, R])

        bank = [ctx.enter_context(nc.psum_tensor(f"bank{k}", [P, BANK], F32)) for k in range(8)]
        out_bank = bank[0:4]
        xt_bank = bank[4:6]
        parts_bank = bank[6]
        spread_bank = bank[7]
        bx_cols = spread_bank[:, 0:P]
        h_cols = spread_bank[:, P : P + C]

        ids_in = sem("ids_in")
        ids_all_in = sem("ids_all_in")
        w_in = sem("w_in")
        clamped = sem("clamped")
        offsets_ready = sem("offsets_ready")
        mask_steps = sem("mask_steps")
        ident_steps = sem("ident_steps")
        ident_ready = sem("ident_ready")
        ident2_ready = sem("ident2_ready")
        m_table_ready = sem("m_table_ready")
        a_raw_in = [sem(f"a_raw_in{k}") for k in range(A_RAWS)]
        b_raw_in = [sem(f"b_raw_in{k}") for k in range(2)]
        b_turned = sem("b_turned")
        b_moved = sem("b_moved")
        a_turned = sem("a_turned")
        a_lower = sem("a_lower")
        a_upper = sem("a_upper")
        x_in = [sem(f"x_in{k}") for k in range(UNROLL)]
        stored = [sem(f"stored{k}") for k in range(UNROLL)]
        xt_done = sem("xt_done")
        xt_moved = sem("xt_moved")
        b_staged = sem("b_staged")
        m_staged = sem("m_staged")
        slab_staged = sem("slab_staged")
        parts_done = sem("parts_done")
        parts_moved = sem("parts_moved")
        bx_done = sem("bx_done")
        bx_summed = sem("bx_summed")
        spread_ready = sem("spread_ready")
        h_done = sem("h_done")
        h_moved = sem("h_moved")
        out_done = sem("out_done")
        out_moved = sem("out_moved")

        block = ctx.enter_context(nc.Block())

        def pairs(engine, step, first=0, last=0):
            turns = PAIRS // UNROLL
            for turn in range(first):
                for slot in range(UNROLL):
                    step(turn * UNROLL + slot, slot, turn)
            with engine.Fori(first, turns - last) as turn:
                for slot in range(UNROLL):
                    step(turn * UNROLL + slot, slot, turn)
            for turn in range(turns - last, turns):
                for slot in range(UNROLL):
                    step(turn * UNROLL + slot, slot, turn)

        @block.sync
        def _(sp):
            sp.dma_start(ids[:, 0, :], cond_ids.rearrange("(o n) -> o n", o=1)).then_inc(ids_in, 16)
            sp.dma_start(ids[:, 1, :], adapter_ids.rearrange("(o n) -> o n", o=1)).then_inc(ids_in, 16)

            def load_b(n):
                k = n % 2
                wait(sp, b_turned, (n - 1) * 4)
                sp.dma_start(b_raw[:, k, :, :], b_loads[n]).then_inc(b_raw_in[k], 16)

            def load_x(pair, slot, turn):
                wait(sp, out_done, (pair - UNROLL + 1) * HALVES)
                sp.dma_start(moving[0:C, slot, 0, :], x_pairs[pair, 0]).then_inc(x_in[slot], 16)
                sp.dma_start(moving[C:P, slot, 1, :], x_pairs[pair, 1]).then_inc(x_in[slot], 16)

            def store(pair, slot, turn):
                sp.wait_ge(out_moved, (pair + 1) * HALVES)
                sp.dma_start(out_pairs[pair], result[:, slot, :]).then_inc(stored[slot], 16)

            load_b(0)
            load_b(1)
            sp.dma_start(m_table[0:C, :, :], cond_w.rearrange("w c d -> c w d")).then_inc(w_in, 16)
            sp.dma_start(m_table[C:P, :, :], cond_w.rearrange("w c d -> c w d")).then_inc(w_in, 16)
            sp.dma_start(ids_all[:, :], adapter_ids.partition_broadcast(P)).then_inc(ids_all_in, 16)
            load_x(0, 0, 0)
            load_x(1, 1, 0)
            for n in range(2, GROUPS // 2):
                load_b(n)
            load_x(2, 2, 0)
            load_x(3, 3, 0)
            with sp.Fori(1, PAIRS // UNROLL) as turn:
                for slot in range(UNROLL):
                    load_x(turn * UNROLL + slot, slot, turn)
                    store((turn - 1) * UNROLL + slot, slot, turn)
            for slot in range(UNROLL):
                store(PAIRS - UNROLL + slot, slot, 0)
            for slot in range(UNROLL):
                sp.wait_ge(stored[slot], 16 * (PAIRS // UNROLL))

        @block.gpsimd
        def _(pool):
            nc.gpsimd.memset(ident[:, :], 0.0).then_inc(ident_steps, 1)
            pool.wait_ge(ident_steps, 1)
            nc.gpsimd.affine_select(
                out=ident[:, :], in_=ident[:, :], compare_op=ALU.not_equal, fill=1.0, base=0,
                pattern=[[-1, P]], channel_multiplier=1,
            ).then_inc(ident_ready, 1)

            for g in range(GROUPS):
                k = g % A_RAWS
                wait(pool, a_turned, g - A_RAWS + 1)
                for q in range(QUADS):
                    pool.dma_start(a_raw[32 * q : 32 * q + 32, k, :, :], a_loads[g, q]).then_inc(a_raw_in[k], 16)

            pool.wait_ge(offsets_ready, 3)
            pool.wait_ge(m_table_ready, 1)
            pool.wait_ge(b_moved, 2 * GROUPS)

            def place(kind, batch, last):
                return nc.values_load(
                    offsets[:, kind, bass.ds(batch, 1)], engines=[mybir.EngineType.Pool], min_val=0, max_val=last,
                    skip_runtime_bounds_check_because="the ids are clamped before offsets are worked out",
                )

            def stage(pair, slot, turn):
                a = [place(2, 2 * pair + h, (ADAPTERS - 1) * R) for h in range(2)]
                w = [place(0, 2 * pair + h, (CONDS - 1) * C) for h in range(2)]
                bt = bt_table[:, :, :, :].rearrange("p j a r -> p j (a r)")
                m = m_table[:, :, :].rearrange("p w d -> p (w d)")
                wait(pool, parts_done, pair - UNROLL + 1)
                for h in range(2):
                    nc.gpsimd.tensor_copy(b_pair[:, slot, :, h, :], bt[:, :, bass.ds(a[h], R)]).then_inc(b_staged, 1)
                wait(pool, out_done, (pair - UNROLL + 1) * HALVES)
                pool.wait_ge(b_staged, 2 * (pair + 1))
                nc.gpsimd.tensor_copy(weights[0:C, slot, 0, :], m[0:C, bass.ds(w[0], C)]).then_inc(m_staged, 1)
                pool.wait_ge(m_staged, 2 * pair + 1)
                nc.gpsimd.tensor_copy(weights[C:P, slot, 1, :], m[C:P, bass.ds(w[1], C)]).then_inc(m_staged, 1)
                pool.wait_ge(m_staged, 2 * pair + 2)

            pairs(pool, stage, first=1)

        @block.scalar
        def _(act):
            with act.Fori(0, GROUPS // TABLE_UNROLL) as turn:
                for k in range(TABLE_UNROLL):
                    g = turn * TABLE_UNROLL + k
                    for u in range(2):
                        act.wait_ge(b_turned, 2 * g + u + 1)
                        nc.scalar.copy(
                            bt_table[:, 4 * u : 4 * u + 4, :, :].rearrange("p j a r -> p j (a r)")[:, :, bass.ds(g * P, P)],
                            bank[2 * k + u][:, :].rearrange("p (j c) -> p j c", c=P),
                        ).then_inc(b_moved, 1)
                    act.wait_ge(a_turned, g + 1)
                    nc.scalar.copy(
                        at_table[C:P, bass.ds(2 * g + 1, 1), :], at_table[0:C, bass.ds(2 * g, 1), :]
                    ).then_inc(a_upper, 1)

            def move_x(pair, slot, half):
                act.wait_ge(xt_done, 2 * pair + half + 1)
                nc.scalar.copy(
                    x_t[:, slot % 2, :, half * C : half * C + C],
                    xt_bank[half][:, :].rearrange("p (j c) -> p j c", c=C),
                ).then_inc(xt_moved, 1)

            def move_out(pair, slot, half):
                act.wait_ge(out_done, HALVES * pair + half + 1)
                nc.scalar.copy(
                    result[:, slot, half * BANK : (half + 1) * BANK], out_bank[2 * (slot % 2) + half][:, :]
                ).then_inc(out_moved, 1)

            def move(pair, slot, turn):
                ahead = (slot + 2) % UNROLL
                last = isinstance(pair, int) and pair + 2 >= PAIRS
                if not last:
                    move_x(pair + 2, ahead, 0)
                if half_wait(turn):
                    act.wait_ge(stored[slot], 16 * turn)
                move_out(pair, slot, 0)
                if not last:
                    move_x(pair + 2, ahead, 1)
                move_out(pair, slot, 1)

            def half_wait(turn):
                return not isinstance(turn, int) or turn > 0

            for pair in range(2):
                for half in range(2):
                    move_x(pair, pair, half)
            pairs(act, move, first=1, last=1)

        @block.vector
        def _(dve):
            dve.wait_ge(ids_in, 32)
            nc.vector.tensor_scalar(offsets[:, 1, :], ids[:, 0, :], 0, CONDS - 1, ALU.max, ALU.min).then_inc(clamped, 1)
            nc.vector.tensor_scalar(ids[:, 1, :], ids[:, 1, :], 0, ADAPTERS - 1, ALU.max, ALU.min).then_inc(clamped, 1)
            dve.wait_ge(clamped, 2)
            nc.vector.tensor_scalar(offsets[:, 0, :], offsets[:, 1, :], C, None, ALU.mult).then_inc(offsets_ready, 1)
            nc.vector.tensor_scalar(offsets[:, 2, :], ids[:, 1, :], R, None, ALU.mult).then_inc(offsets_ready, 1)
            nc.vector.tensor_scalar(in_slab_row[:, :], ids[:, 1, :], PER_SLAB - 1, None, ALU.bitwise_and).then_inc(clamped, 1)
            dve.wait_ge(clamped, 3)
            nc.vector.tensor_tensor(slab_row[:, :], ids[:, 1, :], in_slab_row[:, :], ALU.subtract).then_inc(clamped, 1)
            dve.wait_ge(clamped, 4)
            of_even = slab_row[:, :].rearrange("o (n h) -> o h n", h=2)[:, 0]
            nc.vector.tensor_scalar(of_even, of_even, PER_SLAB, None, ALU.bitwise_xor).then_inc(clamped, 1)
            dve.wait_ge(clamped, 5)
            nc.vector.tensor_scalar(offsets[:, 3, :], slab_row[:, :], T // PER_SLAB, None, ALU.mult).then_inc(offsets_ready, 1)

            dve.wait_ge(ident_ready, 1)
            nc.vector.tensor_tensor(ident2[:, :], ident[:, 0:C], ident[:, C:P], ALU.add).then_inc(ident2_ready, 1)
            dve.wait_ge(ident2_ready, 1)
            dve.wait_ge(w_in, 32)
            nc.vector.tensor_tensor(
                m_table[:, :, :], m_table[:, :, :], ident2[:, :].unsqueeze(1).to_broadcast([P, CONDS, C]), ALU.add
            ).then_inc(m_table_ready, 1)

            dve.wait_ge(ids_all_in, 16)
            nc.vector.tensor_scalar(ids_all[:, :], ids_all[:, :], 0, ADAPTERS - 1, ALU.max, ALU.min).then_inc(mask_steps, 1)
            dve.wait_ge(mask_steps, 1)
            nc.vector.tensor_scalar(in_slab[:, :], ids_all[:, :], PER_SLAB - 1, None, ALU.bitwise_and).then_inc(mask_steps, 1)
            dve.wait_ge(mask_steps, 2)
            own = in_slab[:, :].rearrange("p (n h) -> p h n", h=2)
            for h in range(2):
                rows = slice(h * C, h * C + C)
                for k in range(PER_SLAB):
                    nc.vector.tensor_scalar(slab_mask[rows, :, k], own[rows, h, :], k, None, ALU.is_equal).then_inc(
                        mask_steps, 1
                    )
            dve.wait_ge(mask_steps, 2 + 2 * PER_SLAB)

            for g in range(GROUPS):
                dve.wait_ge(a_raw_in[g % A_RAWS], 16 * QUADS * (g // A_RAWS + 1))
                nc.vector.transpose(
                    at_table[:, 2 * g, :].rearrange("p (w s) -> p s w", s=32),
                    a_raw[:, g % A_RAWS, :, :].rearrange("p e (s r) -> p s e r", r=R),
                ).then_inc(a_turned, 1)
                dve.wait_ge(a_turned, g + 1)
                nc.vector.tensor_copy(at_table[0:C, 2 * g + 1, :], at_table[C:P, 2 * g, :]).then_inc(a_lower, 1)
            dve.wait_ge(a_lower, GROUPS)
            dve.wait_ge(a_upper, GROUPS)
            dve.wait_ge(offsets_ready, 3)

            def stage_slab(pair, slot, h):
                at = nc.values_load(
                    offsets[:, 3, bass.ds(2 * pair + h, 1)], engines=[mybir.EngineType.DVE], min_val=0,
                    max_val=(SLABS - 1) * T,
                    skip_runtime_bounds_check_because="the ids are clamped before offsets are worked out",
                )
                rows = slice(C, P) if h == 0 else slice(0, C)
                wait(dve, out_done, (pair - UNROLL + 1) * HALVES)
                nc.vector.tensor_copy(
                    moving[rows, slot, h, :], at_table[rows, :, :].rearrange("p s t -> p (s t)")[:, bass.ds(at, T)]
                ).then_inc(slab_staged, 1)

            def parts(pair):
                dve.wait_ge(parts_done, pair + 1)
                nc.vector.tensor_copy(bx_parts[:, :], parts_bank[:, 0:P]).then_inc(parts_moved, 1)

            def spread(pair):
                dve.wait_ge(bx_done, pair + 1)
                for h in range(2):
                    rows = slice(h * C, h * C + C)
                    nc.vector.tensor_reduce(
                        bx[rows, :],
                        bx_cols[rows, :].rearrange("p (q h r) -> p h r q", q=QUADS, h=2)[:, h],
                        AX_X, ALU.add,
                    ).then_inc(bx_summed, 1)
                dve.wait_ge(bx_summed, 2 * (pair + 1))
                nc.vector.tensor_tensor(
                    bx_spread[:, :, :],
                    bx[:, :].unsqueeze(1).to_broadcast([P, PER_SLAB, R]),
                    slab_mask[:, bass.ds(pair, 1), :].rearrange("p o k -> p (o k)").unsqueeze(2).to_broadcast([P, PER_SLAB, R]),
                    ALU.mult,
                ).then_inc(spread_ready, 1)

            def move_h(pair, slot):
                dve.wait_ge(h_done, pair + 1)
                nc.vector.tensor_copy(weights[C:P, slot, 0, :], h_cols[C:P, :]).then_inc(h_moved, 1)
                nc.vector.tensor_copy(weights[0:C, slot, 1, :], h_cols[0:C, :]).then_inc(h_moved, 1)

            def step(pair, slot, turn):
                ahead = (slot + 1) % UNROLL
                if isinstance(pair, int) and pair + 1 >= PAIRS:
                    return
                parts(pair + 1)
                stage_slab(pair + 1, ahead, 0)
                spread(pair + 1)
                stage_slab(pair + 1, ahead, 1)
                move_h(pair + 1, ahead)

            parts(0)
            stage_slab(0, 0, 0)
            spread(0)
            stage_slab(0, 0, 1)
            move_h(0, 0)
            pairs(dve, step, first=1, last=1)

        @block.tensor
        def _(pe):
            pe.wait_ge(ident_ready, 1)

            with pe.Fori(0, GROUPS // TABLE_UNROLL) as turn:
                for k in range(TABLE_UNROLL):
                    if k % 2 == 0:
                        pe.wait_ge(b_raw_in[k // 2], 16 * (turn + 1))
                    for u in range(2):
                        for j in range(4):
                            done = nc.tensor.transpose(
                                bank[2 * k + u][:, j * P : (j + 1) * P],
                                b_raw[:, k // 2, k % 2, (4 * u + j) * P : (4 * u + j + 1) * P],
                                ident[:, :],
                            )
                        done.then_inc(b_turned, 1)
                pe.wait_ge(b_moved, 2 * TABLE_UNROLL * (turn + 1))

            def arrived(slot, turn):
                pe.wait_ge(x_in[slot], 32 * (turn + 1))

            def transpose_x(slot, half):
                rows = slice(half * C, half * C + C)
                for j in range(CHUNKS):
                    done = nc.tensor.transpose(
                        xt_bank[half][:, j * C : (j + 1) * C],
                        moving[rows, slot, half, j * P : (j + 1) * P],
                        ident[rows, rows],
                    )
                done.then_inc(xt_done, 1)

            def project(pair, slot):
                pe.wait_ge(xt_moved, 2 * (pair + 1))
                pe.wait_ge(b_staged, 2 * (pair + 1))
                for j in range(CHUNKS):
                    q = j % QUADS
                    done = nc.tensor.matmul(
                        parts_bank[32 * q : 32 * q + 32, 0:P],
                        b_pair[:, slot, j, :, :].rearrange("p h r -> p (h r)"),
                        x_t[:, slot % 2, j, :],
                        start=j < QUADS, stop=j >= QUADS,
                    )
                done.then_inc(parts_done, 1)

            def turn_parts(pair):
                pe.wait_ge(parts_moved, pair + 1)
                nc.tensor.transpose(bx_cols, bx_parts[:, :], ident[:, :]).then_inc(bx_done, 1)

            def apply_m(pair, slot):
                pe.wait_ge(m_table_ready, 1)
                pe.wait_ge(spread_ready, pair + 1)
                pe.wait_ge(m_staged, 2 * (pair + 1))
                for h in range(2):
                    rows = slice(h * C, h * C + C)
                    to = slice(C, P) if h == 0 else slice(0, C)
                    done = nc.tensor.matmul(
                        h_cols[to, :],
                        bx_spread[rows, :, :].rearrange("p k r -> p (k r)"),
                        weights[rows, slot, h, :],
                        start=True, stop=True,
                    )
                done.then_inc(h_done, 1)

            def multiply(pair, slot, half):
                if half == 0:
                    pe.wait_ge(slab_staged, 2 * (pair + 1))
                    pe.wait_ge(h_moved, 2 * (pair + 1))
                wait(pe, out_moved, 2 * (pair - 2) + half + 1)
                for h in range(2):
                    done = nc.tensor.matmul(
                        out_bank[2 * (slot % 2) + half][h * C : h * C + C, :],
                        weights[:, slot, h, :],
                        moving[:, slot, h, half * BANK : (half + 1) * BANK],
                        start=True, stop=True,
                    )
                done.then_inc(out_done, 1)

            def step(pair, slot, turn):
                one = (slot + 1) % UNROLL
                two = (slot + 2) % UNROLL
                static = isinstance(pair, int)
                if not static or pair + 2 < PAIRS:
                    arrived(two, turn + (slot + 2) // UNROLL)
                if not static or pair + 1 < PAIRS:
                    project(pair + 1, one)
                if not static or pair + 2 < PAIRS:
                    transpose_x(two, 0)
                multiply(pair, slot, 0)
                if not static or pair + 1 < PAIRS:
                    turn_parts(pair + 1)
                if not static or pair + 2 < PAIRS:
                    transpose_x(two, 1)
                multiply(pair, slot, 1)
                if not static or pair + 1 < PAIRS:
                    apply_m(pair + 1, one)

            arrived(0, 0)
            transpose_x(0, 0)
            transpose_x(0, 1)
            arrived(1, 0)
            project(0, 0)
            transpose_x(1, 0)
            turn_parts(0)
            transpose_x(1, 1)
            apply_m(0, 0)
            pairs(pe, step, first=1, last=1)


_INS = ["x", "itok_B_0_15", "itok_B_4_50", "L0_cond_weights", "L1_cond_A", "L1_cond_B"]


def kernel(**inputs):
    import numpy as _np
    import concourse.bacc as _bacc
    from concourse import mybir as _mybir
    from concourse.bass_utils import run_bass_kernel_spmd as _run

    nc = _bacc.Bacc("TRN2", target_bir_lowering=False, num_devices=1)
    arrays, args = {}, []
    for name in _INS:
        a = _np.ascontiguousarray(inputs[name])
        arrays[f"in_{name}"] = a
        args.append(nc.dram_tensor(f"in_{name}", a.shape, _mybir.dt.from_np(a.dtype), kind="ExternalInput").ap())
    out = nc.dram_tensor("out_0", arrays["in_x"].shape, _mybir.dt.float32, kind="ExternalOutput").ap()
    cond_lora_kernel(nc, *args, out)
    r = _run(nc, [arrays], core_ids=[0])
    return r.results[0]["out_0"]
```

```python
from contextlib import ExitStack

import concourse.bass as bass
from concourse import mybir

F32 = mybir.dt.float32
I32 = mybir.dt.int32
ALU = mybir.AluOpType
AX_X = mybir.AxisListType.X

P = 128
UNROLL = 4
A_RAWS = 4
M_AT, B_AT, A_AT = range(3)
TABLE_UNROLL = 4


def wait(engine, semaphore, value):
    if not isinstance(value, int) or value > 0:
        engine.wait_ge(semaphore, value)


def cond_lora_kernel(nc, x, cond_ids, adapter_ids, cond_w, lora_a, lora_b, out):
    BATCH, C, T = x.shape
    CONDS = cond_w.shape[0]
    ADAPTERS, _, R = lora_a.shape
    PAIRS = BATCH // 2
    CHUNKS = T // P
    BANK = 512
    HALVES = T // BANK
    PER_SLAB = C // R
    SLABS = ADAPTERS // PER_SLAB
    PER_GROUP = P // R
    GROUPS = ADAPTERS // PER_GROUP
    QUADS = 4
    assert 2 * C == P and 2 * R * QUADS == P and CHUNKS == 2 * QUADS and HALVES == 2
    assert PAIRS % UNROLL == 0 and GROUPS % TABLE_UNROLL == 0 and CONDS * C == T

    a_loads = lora_a.rearrange("(g q e) (w s) r -> g q w e (s r)", q=QUADS, e=2, s=32)
    b_loads = lora_b.rearrange("(l g a) r t -> l (a r) g t", g=2, a=PER_GROUP)
    x_pairs = x.rearrange("(n a) c t -> n a c t", a=2)
    out_pairs = out.rearrange("(n a) c t -> n (a c) t", a=2)

    with ExitStack() as ctx:

        def sb(name, shape, dtype=F32):
            return ctx.enter_context(nc.sbuf_tensor(name, shape, dtype))

        def sem(name):
            return ctx.enter_context(nc.semaphore(name))

        at_table = sb("at_table", [P, SLABS, T])
        bt_table = sb("bt_table", [P, CHUNKS, ADAPTERS, R])
        m_table = sb("m_table", [P, CONDS, C])
        ident = sb("ident", [P, P])
        ident2 = sb("ident2", [P, C])
        ids = sb("ids", [1, 2, BATCH], I32)
        offsets = sb("offsets", [1, 3, BATCH], I32)
        cond_row = sb("cond_row", [1, BATCH], I32)
        in_slab_row = sb("in_slab_row", [1, BATCH], I32)
        slab_row = sb("slab_row", [1, BATCH], I32)
        ids_all = sb("ids_all", [P, BATCH], I32)
        in_slab = sb("in_slab", [P, BATCH], I32)
        slab_mask = sb("slab_mask", [P, PAIRS, PER_SLAB])

        a_raw = sb("a_raw", [P, A_RAWS, 2, 32 * R])
        b_raw = sb("b_raw", [P, 2, 2, T])

        moving = sb("moving", [P, UNROLL, 2, T])
        weights = sb("weights", [P, UNROLL, 2, C])
        b_pair = sb("b_pair", [P, UNROLL, CHUNKS, 2, R])
        x_t = sb("x_t", [P, 2, CHUNKS, P])
        result = sb("result", [P, UNROLL, T])
        bx_parts = sb("bx_parts", [P, P])
        bx = sb("bx", [P, R])
        bx_spread = sb("bx_spread", [P, PER_SLAB, R])

        bank = [ctx.enter_context(nc.psum_tensor(f"bank{k}", [P, BANK], F32)) for k in range(8)]
        out_bank = bank[0:4]
        xt_bank = bank[4:6]
        parts_bank = bank[6]
        spread_bank = bank[7]
        bx_cols = spread_bank[:, 0:P]
        h_cols = spread_bank[:, P : P + C]

        ids_in = sem("ids_in")
        ids_all_in = sem("ids_all_in")
        w_in = sem("w_in")
        clamped = sem("clamped")
        offsets_ready = sem("offsets_ready")
        mask_steps = sem("mask_steps")
        ident_steps = sem("ident_steps")
        ident_ready = sem("ident_ready")
        ident2_ready = sem("ident2_ready")
        m_table_ready = sem("m_table_ready")
        a_raw_in_sp = [sem(f"a_raw_in_sp{k}") for k in range(A_RAWS)]
        a_raw_in_pool = [sem(f"a_raw_in_pool{k}") for k in range(A_RAWS)]
        b_raw_in = [sem(f"b_raw_in{k}") for k in range(2)]
        b_turned = sem("b_turned")
        b_moved = sem("b_moved")
        a_turned = sem("a_turned")
        a_lower = sem("a_lower")
        a_upper = sem("a_upper")
        x_in = [sem(f"x_in{k}") for k in range(UNROLL)]
        stored = [sem(f"stored{k}") for k in range(UNROLL)]
        xt_done = sem("xt_done")
        xt_moved = sem("xt_moved")
        b_staged = sem("b_staged")
        m_staged = sem("m_staged")
        slab_staged = sem("slab_staged")
        parts_done = sem("parts_done")
        parts_moved = sem("parts_moved")
        bx_done = sem("bx_done")
        bx_summed = sem("bx_summed")
        spread_ready = sem("spread_ready")
        h_done = sem("h_done")
        h_moved = sem("h_moved")
        out_done = sem("out_done")
        out_moved = sem("out_moved")

        block = ctx.enter_context(nc.Block())

        def pairs(engine, step, first=0, last=0):
            turns = PAIRS // UNROLL
            for turn in range(first):
                for slot in range(UNROLL):
                    step(turn * UNROLL + slot, slot, turn)
            with engine.Fori(first, turns - last) as turn:
                for slot in range(UNROLL):
                    step(turn * UNROLL + slot, slot, turn)
            for turn in range(turns - last, turns):
                for slot in range(UNROLL):
                    step(turn * UNROLL + slot, slot, turn)

        def place(engine, kind, batch, last):
            return nc.values_load(
                offsets[:, kind, bass.ds(batch, 1)], engines=[engine], min_val=0, max_val=last,
                skip_runtime_bounds_check_because="the ids are clamped before the places are worked out",
            )

        def load_a(engine, g, blocks, arrived):
            k = g % A_RAWS
            wait(engine, a_turned, g - A_RAWS + 1)
            for q in blocks:
                engine.dma_start(a_raw[32 * q : 32 * q + 32, k, :, :], a_loads[g, q]).then_inc(arrived[k], 16)

        @block.sync
        def _(sp):
            def load_b(n):
                k = n % 2
                wait(sp, b_turned, (n - 1) * 4)
                sp.dma_start(b_raw[:, k, :, :], b_loads[n]).then_inc(b_raw_in[k], 16)

            def load_x(pair, slot, turn):
                wait(sp, out_done, (pair - UNROLL + 1) * HALVES)
                sp.dma_start(moving[0:C, slot, 0, :], x_pairs[pair, 0]).then_inc(x_in[slot], 16)
                sp.dma_start(moving[C:P, slot, 1, :], x_pairs[pair, 1]).then_inc(x_in[slot], 16)

            def store(pair, slot, turn):
                sp.wait_ge(out_moved, (pair + 1) * HALVES)
                sp.dma_start(out_pairs[pair], result[:, slot, :]).then_inc(stored[slot], 16)

            load_b(0)
            load_b(1)
            load_a(sp, 0, (0, 1), a_raw_in_sp)
            load_b(2)
            load_a(sp, 1, (0, 1), a_raw_in_sp)
            load_b(3)
            for g in range(2, GROUPS):
                load_a(sp, g, (0, 1), a_raw_in_sp)
                if g == GROUPS - 3:
                    load_x(0, 0, 0)
            for slot in range(1, UNROLL):
                load_x(slot, slot, 0)
            with sp.Fori(1, PAIRS // UNROLL) as turn:
                for slot in range(UNROLL):
                    load_x(turn * UNROLL + slot, slot, turn)
                    store((turn - 1) * UNROLL + slot, slot, turn)
            for slot in range(UNROLL):
                store(PAIRS - UNROLL + slot, slot, 0)
            for slot in range(UNROLL):
                sp.wait_ge(stored[slot], 16 * (PAIRS // UNROLL))

        @block.gpsimd
        def _(pool):
            nc.gpsimd.memset(ident[:, :], 0.0).then_inc(ident_steps, 1)
            pool.wait_ge(ident_steps, 1)
            nc.gpsimd.affine_select(
                out=ident[:, :], in_=ident[:, :], compare_op=ALU.not_equal, fill=1.0, base=0,
                pattern=[[-1, P]], channel_multiplier=1,
            ).then_inc(ident_ready, 1)

            for g in range(GROUPS):
                load_a(pool, g, (2, 3), a_raw_in_pool)

            pool.wait_ge(offsets_ready, 3)
            pool.wait_ge(b_moved, 2 * GROUPS)

            def stage(pair, slot, turn):
                at = [place(mybir.EngineType.Pool, B_AT, 2 * pair + h, (ADAPTERS - 1) * R) for h in range(2)]
                wait(pool, parts_done, pair - UNROLL + 1)
                for h in range(2):
                    nc.gpsimd.tensor_copy(
                        b_pair[:, slot, :, h, :],
                        bt_table[:, :, :, :].rearrange("p j a r -> p j (a r)")[:, :, bass.ds(at[h], R)],
                    ).then_inc(b_staged, 1)

            pairs(pool, stage, first=1)

        @block.scalar
        def _(act):
            act.dma_start(ids[:, 0, :], cond_ids.rearrange("(o n) -> o n", o=1)).then_inc(ids_in, 16)
            act.dma_start(ids[:, 1, :], adapter_ids.rearrange("(o n) -> o n", o=1)).then_inc(ids_in, 16)
            act.dma_start(ids_all[:, :], adapter_ids.partition_broadcast(P)).then_inc(ids_all_in, 16)
            act.dma_start(m_table[0:C, :, :], cond_w.rearrange("w c d -> c w d")).then_inc(w_in, 16)

            with act.Fori(0, GROUPS // TABLE_UNROLL) as turn:
                for k in range(TABLE_UNROLL):
                    g = turn * TABLE_UNROLL + k
                    for u in range(2):
                        act.wait_ge(b_turned, 2 * g + u + 1)
                        nc.scalar.copy(
                            bt_table[:, 4 * u : 4 * u + 4, :, :].rearrange("p j a r -> p j (a r)")[:, :, bass.ds(g * P, P)],
                            bank[2 * k + u][:, :].rearrange("p (j c) -> p j c", c=P),
                        ).then_inc(b_moved, 1)

            def copy_upper(g):
                act.wait_ge(a_turned, g + 1)
                nc.scalar.copy(at_table[C:P, 2 * g + 1, :], at_table[0:C, 2 * g, :]).then_inc(a_upper, 1)

            def move_x(pair, slot, half):
                act.wait_ge(xt_done, 2 * pair + half + 1)
                nc.scalar.copy(
                    x_t[:, slot % 2, :, half * C : half * C + C],
                    xt_bank[half][:, :].rearrange("p (j c) -> p j c", c=C),
                ).then_inc(xt_moved, 1)

            def move_out(pair, slot, half):
                act.wait_ge(out_done, HALVES * pair + half + 1)
                nc.scalar.copy(
                    result[:, slot, half * BANK : (half + 1) * BANK], out_bank[2 * (slot % 2) + half][:, :]
                ).then_inc(out_moved, 1)

            def stage_m(pair, slot):
                m = m_table[:, :, :].rearrange("p w d -> p (w d)")
                at = [place(mybir.EngineType.Activation, M_AT, 2 * pair + h, (CONDS - 1) * C) for h in range(2)]
                wait(act, out_done, (pair - UNROLL + 1) * HALVES)
                nc.scalar.copy(weights[0:C, slot, 0, :], m[0:C, bass.ds(at[0], C)]).then_inc(m_staged, 1)
                nc.scalar.copy(weights[C:P, slot, 1, :], m[C:P, bass.ds(at[1], C)]).then_inc(m_staged, 1)

            def move(pair, slot, turn):
                ahead = (slot + 2) % UNROLL
                last = isinstance(pair, int) and pair + 2 >= PAIRS
                if not last:
                    move_x(pair + 2, ahead, 0)
                if half_wait(turn):
                    act.wait_ge(stored[slot], 16 * turn)
                move_out(pair, slot, 0)
                if not last:
                    move_x(pair + 2, ahead, 1)
                    stage_m(pair + 2, ahead)
                move_out(pair, slot, 1)

            def half_wait(turn):
                return not isinstance(turn, int) or turn > 0

            for g in range(GROUPS - 2):
                copy_upper(g)
            act.wait_ge(offsets_ready, 3)
            act.wait_ge(m_table_ready, 2)
            for pair in range(2):
                for half in range(2):
                    move_x(pair, pair, half)
                stage_m(pair, pair)
                copy_upper(GROUPS - 2 + pair)
            pairs(act, move, first=1, last=1)

        @block.vector
        def _(dve):
            dve.wait_ge(ids_in, 32)
            nc.vector.tensor_scalar(cond_row[:, :], ids[:, 0, :], 0, CONDS - 1, ALU.max, ALU.min).then_inc(clamped, 1)
            nc.vector.tensor_scalar(ids[:, 1, :], ids[:, 1, :], 0, ADAPTERS - 1, ALU.max, ALU.min).then_inc(clamped, 1)
            dve.wait_ge(clamped, 2)
            nc.vector.tensor_scalar(offsets[:, M_AT, :], cond_row[:, :], C, None, ALU.mult).then_inc(offsets_ready, 1)
            nc.vector.tensor_scalar(offsets[:, B_AT, :], ids[:, 1, :], R, None, ALU.mult).then_inc(offsets_ready, 1)
            nc.vector.tensor_scalar(in_slab_row[:, :], ids[:, 1, :], PER_SLAB - 1, None, ALU.bitwise_and).then_inc(clamped, 1)
            dve.wait_ge(clamped, 3)
            nc.vector.tensor_tensor(slab_row[:, :], ids[:, 1, :], in_slab_row[:, :], ALU.subtract).then_inc(clamped, 1)
            dve.wait_ge(clamped, 4)
            of_even = slab_row[:, :].rearrange("o (n h) -> o h n", h=2)[:, 0]
            nc.vector.tensor_scalar(of_even, of_even, PER_SLAB, None, ALU.bitwise_xor).then_inc(clamped, 1)
            dve.wait_ge(clamped, 5)
            nc.vector.tensor_scalar(offsets[:, A_AT, :], slab_row[:, :], T // PER_SLAB, None, ALU.mult).then_inc(offsets_ready, 1)

            dve.wait_ge(ident_ready, 1)
            nc.vector.tensor_tensor(ident2[:, :], ident[:, 0:C], ident[:, C:P], ALU.add).then_inc(ident2_ready, 1)
            dve.wait_ge(ident2_ready, 1)
            dve.wait_ge(w_in, 16)
            for n, rows in enumerate((slice(C, P), slice(0, C))):
                wait(dve, m_table_ready, n)
                nc.vector.tensor_tensor(
                    m_table[rows, :, :], m_table[0:C, :, :],
                    ident2[0:C, :].unsqueeze(1).to_broadcast([C, CONDS, C]), ALU.add,
                ).then_inc(m_table_ready, 1)

            dve.wait_ge(ids_all_in, 16)
            nc.vector.tensor_scalar(ids_all[:, :], ids_all[:, :], 0, ADAPTERS - 1, ALU.max, ALU.min).then_inc(mask_steps, 1)
            dve.wait_ge(mask_steps, 1)
            nc.vector.tensor_scalar(in_slab[:, :], ids_all[:, :], PER_SLAB - 1, None, ALU.bitwise_and).then_inc(mask_steps, 1)
            dve.wait_ge(mask_steps, 2)
            own = in_slab[:, :].rearrange("p (n h) -> p h n", h=2)
            for h in range(2):
                rows = slice(h * C, h * C + C)
                for k in range(PER_SLAB):
                    nc.vector.tensor_scalar(slab_mask[rows, :, k], own[rows, h, :], k, None, ALU.is_equal).then_inc(
                        mask_steps, 1
                    )
            dve.wait_ge(mask_steps, 2 + 2 * PER_SLAB)

            for g in range(GROUPS):
                dve.wait_ge(a_raw_in_sp[g % A_RAWS], 32 * (g // A_RAWS + 1))
                dve.wait_ge(a_raw_in_pool[g % A_RAWS], 32 * (g // A_RAWS + 1))
                nc.vector.transpose(
                    at_table[:, 2 * g, :].rearrange("p (w s) -> p s w", s=32),
                    a_raw[:, g % A_RAWS, :, :].rearrange("p e (s r) -> p s e r", r=R),
                ).then_inc(a_turned, 1)
                dve.wait_ge(a_turned, g + 1)
                nc.vector.tensor_copy(at_table[0:C, 2 * g + 1, :], at_table[C:P, 2 * g, :]).then_inc(a_lower, 1)

            def stage_slab(pair, slot, h):
                at = place(mybir.EngineType.DVE, A_AT, 2 * pair + h, (SLABS - 1) * T)
                rows = slice(C, P) if h == 0 else slice(0, C)
                wait(dve, out_done, (pair - UNROLL + 1) * HALVES)
                nc.vector.tensor_copy(
                    moving[rows, slot, h, :], at_table[rows, :, :].rearrange("p s t -> p (s t)")[:, bass.ds(at, T)]
                ).then_inc(slab_staged, 1)

            def parts(pair):
                dve.wait_ge(parts_done, pair + 1)
                nc.vector.tensor_copy(bx_parts[:, :], parts_bank[:, 0:P]).then_inc(parts_moved, 1)

            def spread(pair):
                dve.wait_ge(bx_done, pair + 1)
                for h in range(2):
                    rows = slice(h * C, h * C + C)
                    nc.vector.tensor_reduce(
                        bx[rows, :],
                        bx_cols[rows, :].rearrange("p (q h r) -> p h r q", q=QUADS, h=2)[:, h],
                        AX_X, ALU.add,
                    ).then_inc(bx_summed, 1)
                dve.wait_ge(bx_summed, 2 * (pair + 1))
                nc.vector.tensor_tensor(
                    bx_spread[:, :, :],
                    bx[:, :].unsqueeze(1).to_broadcast([P, PER_SLAB, R]),
                    slab_mask[:, bass.ds(pair, 1), :].rearrange("p o k -> p (o k)").unsqueeze(2).to_broadcast([P, PER_SLAB, R]),
                    ALU.mult,
                ).then_inc(spread_ready, 1)

            def move_h(pair, slot):
                dve.wait_ge(h_done, pair + 1)
                nc.vector.tensor_copy(weights[C:P, slot, 0, :], h_cols[C:P, :]).then_inc(h_moved, 1)
                nc.vector.tensor_copy(weights[0:C, slot, 1, :], h_cols[0:C, :]).then_inc(h_moved, 1)

            def step(pair, slot, turn):
                ahead = (slot + 1) % UNROLL
                if isinstance(pair, int) and pair + 1 >= PAIRS:
                    return
                parts(pair + 1)
                stage_slab(pair + 1, ahead, 0)
                spread(pair + 1)
                stage_slab(pair + 1, ahead, 1)
                move_h(pair + 1, ahead)

            parts(0)
            dve.wait_ge(offsets_ready, 3)
            dve.wait_ge(a_lower, GROUPS)
            dve.wait_ge(a_upper, GROUPS)
            stage_slab(0, 0, 0)
            spread(0)
            stage_slab(0, 0, 1)
            move_h(0, 0)
            pairs(dve, step, first=1, last=1)

        @block.tensor
        def _(pe):
            pe.wait_ge(ident_ready, 1)

            with pe.Fori(0, GROUPS // TABLE_UNROLL) as turn:
                for k in range(TABLE_UNROLL):
                    if k % 2 == 0:
                        pe.wait_ge(b_raw_in[k // 2], 16 * (turn + 1))
                    for u in range(2):
                        for j in range(4):
                            done = nc.tensor.transpose(
                                bank[2 * k + u][:, j * P : (j + 1) * P],
                                b_raw[:, k // 2, k % 2, (4 * u + j) * P : (4 * u + j + 1) * P],
                                ident[:, :],
                            )
                        done.then_inc(b_turned, 1)
                pe.wait_ge(b_moved, 2 * TABLE_UNROLL * (turn + 1))

            def arrived(slot, turn):
                pe.wait_ge(x_in[slot], 32 * (turn + 1))

            def transpose_x(slot, half):
                rows = slice(half * C, half * C + C)
                for j in range(CHUNKS):
                    done = nc.tensor.transpose(
                        xt_bank[half][:, j * C : (j + 1) * C],
                        moving[rows, slot, half, j * P : (j + 1) * P],
                        ident[rows, rows],
                    )
                done.then_inc(xt_done, 1)

            def project(pair, slot):
                pe.wait_ge(xt_moved, 2 * (pair + 1))
                pe.wait_ge(b_staged, 2 * (pair + 1))
                for j in range(CHUNKS):
                    q = j % QUADS
                    done = nc.tensor.matmul(
                        parts_bank[32 * q : 32 * q + 32, 0:P],
                        b_pair[:, slot, j, :, :].rearrange("p h r -> p (h r)"),
                        x_t[:, slot % 2, j, :],
                        start=j < QUADS, stop=j >= QUADS,
                    )
                done.then_inc(parts_done, 1)

            def turn_parts(pair):
                pe.wait_ge(parts_moved, pair + 1)
                nc.tensor.transpose(bx_cols, bx_parts[:, :], ident[:, :]).then_inc(bx_done, 1)

            def apply_m(pair, slot):
                pe.wait_ge(m_table_ready, 2)
                pe.wait_ge(spread_ready, pair + 1)
                pe.wait_ge(m_staged, 2 * (pair + 1))
                for h in range(2):
                    rows = slice(h * C, h * C + C)
                    to = slice(C, P) if h == 0 else slice(0, C)
                    done = nc.tensor.matmul(
                        h_cols[to, :],
                        bx_spread[rows, :, :].rearrange("p k r -> p (k r)"),
                        weights[rows, slot, h, :],
                        start=True, stop=True,
                    )
                done.then_inc(h_done, 1)

            def multiply(pair, slot, half):
                if half == 0:
                    pe.wait_ge(slab_staged, 2 * (pair + 1))
                    pe.wait_ge(h_moved, 2 * (pair + 1))
                wait(pe, out_moved, 2 * (pair - 2) + half + 1)
                for h in range(2):
                    done = nc.tensor.matmul(
                        out_bank[2 * (slot % 2) + half][h * C : h * C + C, :],
                        weights[:, slot, h, :],
                        moving[:, slot, h, half * BANK : (half + 1) * BANK],
                        start=True, stop=True,
                    )
                done.then_inc(out_done, 1)

            def step(pair, slot, turn):
                one = (slot + 1) % UNROLL
                two = (slot + 2) % UNROLL
                static = isinstance(pair, int)
                if not static or pair + 2 < PAIRS:
                    arrived(two, turn + (slot + 2) // UNROLL)
                if not static or pair + 1 < PAIRS:
                    project(pair + 1, one)
                if not static or pair + 2 < PAIRS:
                    transpose_x(two, 0)
                multiply(pair, slot, 0)
                if not static or pair + 1 < PAIRS:
                    turn_parts(pair + 1)
                if not static or pair + 2 < PAIRS:
                    transpose_x(two, 1)
                multiply(pair, slot, 1)
                if not static or pair + 1 < PAIRS:
                    apply_m(pair + 1, one)

            arrived(0, 0)
            transpose_x(0, 0)
            transpose_x(0, 1)
            arrived(1, 0)
            project(0, 0)
            transpose_x(1, 0)
            transpose_x(1, 1)
            turn_parts(0)
            apply_m(0, 0)
            pairs(pe, step, first=1, last=1)


_INS = ["x", "itok_B_0_15", "itok_B_4_50", "L0_cond_weights", "L1_cond_A", "L1_cond_B"]


def kernel(**inputs):
    import numpy as _np
    import concourse.bacc as _bacc
    from concourse import mybir as _mybir
    from concourse.bass_utils import run_bass_kernel_spmd as _run

    nc = _bacc.Bacc("TRN2", target_bir_lowering=False, num_devices=1)
    arrays, args = {}, []
    for name in _INS:
        a = _np.ascontiguousarray(inputs[name])
        arrays[f"in_{name}"] = a
        args.append(nc.dram_tensor(f"in_{name}", a.shape, _mybir.dt.from_np(a.dtype), kind="ExternalInput").ap())
    out = nc.dram_tensor("out_0", arrays["in_x"].shape, _mybir.dt.float32, kind="ExternalOutput").ap()
    cond_lora_kernel(nc, *args, out)
    r = _run(nc, [arrays], core_ids=[0])
    return r.results[0]["out_0"]
```

```python
from contextlib import ExitStack

import concourse.bass as bass
from concourse import mybir

F32 = mybir.dt.float32
I32 = mybir.dt.int32
ALU = mybir.AluOpType

P = 128
A_AFTER_B = ((0,), (1, 2), (3, 4, 5), (6,))
UNROLL = 8
RING = 4
A_RAWS = 4
M_AT, B_AT, A_AT = range(3)
BUSY_BEFORE_B = (18, 4, 8, 18)
BUSY_BEFORE_PAIR = (8, 8, 2)


def wait(engine, semaphore, value):
    if not isinstance(value, int) or value > 0:
        engine.wait_ge(semaphore, value)


def cond_lora_kernel(nc, x, cond_ids, adapter_ids, cond_w, lora_a, lora_b, out):
    BATCH, C, T = x.shape
    CONDS = cond_w.shape[0]
    ADAPTERS, _, R = lora_a.shape
    PAIRS = BATCH // 2
    CHUNKS = T // P
    BANK = 512
    HALVES = T // BANK
    PER_SLAB = C // R
    SLABS = ADAPTERS // PER_SLAB
    PER_GROUP = P // R
    GROUPS = ADAPTERS // PER_GROUP
    QUADS = 4
    assert 2 * C == P and 2 * R * QUADS == P and CHUNKS == 2 * QUADS and HALVES == 2
    assert PAIRS % UNROLL == 0 and CONDS * C == T

    a_loads = lora_a.rearrange("(g e q) (w s) r -> g (q w) e (s r)", q=QUADS, e=2, s=32)
    b_loads = lora_b.rearrange("(l g a) r t -> l (a r) g t", g=2, a=PER_GROUP)
    x_pairs = x.rearrange("(n a) c t -> n a c t", a=2)
    out_pairs = out.rearrange("(n a) c t -> n (a c) t", a=2)

    with ExitStack() as ctx:

        def sb(name, shape, dtype=F32):
            return ctx.enter_context(nc.sbuf_tensor(name, shape, dtype))

        def sem(name):
            return ctx.enter_context(nc.semaphore(name))

        at_table = sb("at_table", [P, SLABS, T])
        bt_table = sb("bt_table", [P, CHUNKS, ADAPTERS, R])
        m_table = sb("m_table", [P, CONDS, C])
        ident = sb("ident", [P, P])
        ident4 = sb("ident4", [P, 2 * R])
        ident2 = sb("ident2", [P, C])
        ids = sb("ids", [1, 2, BATCH], I32)
        offsets = sb("offsets", [1, 3, BATCH], I32)
        cond_row = sb("cond_row", [1, BATCH], I32)
        group_row = sb("group_row", [1, BATCH], I32)
        slab_row = sb("slab_row", [1, BATCH], I32)
        ids_all = sb("ids_all", [P, BATCH], I32)
        in_slab = sb("in_slab", [P, BATCH], I32)
        slab_mask = sb("slab_mask", [P, PAIRS, PER_SLAB])

        moving = sb("moving", [P, UNROLL, 2, T])
        a_raw = moving[:, RING : RING + 2, :, :].rearrange("p n h (e c) -> p (n h) e c", e=2)
        b_raw = moving[:, RING + 2 : RING + 4, :, :]
        weights = sb("weights", [P, RING, 2, C])
        b_pair = sb("b_pair", [P, RING, CHUNKS, 2, R])
        x_t = sb("x_t", [P, 2, CHUNKS, P])
        result = sb("result", [P, RING, T])
        bx_parts = sb("bx_parts", [P, P])
        bx_spread = sb("bx_spread", [P, PER_SLAB, R])

        bank = [ctx.enter_context(nc.psum_tensor(f"bank{k}", [P, BANK], F32)) for k in range(8)]
        out_bank = bank[0:4]
        xt_bank = bank[4:6]
        parts_bank = bank[6]
        spread_bank = bank[7]
        bx_cols = spread_bank[:, 0:R]
        h_cols = spread_bank[:, P : P + C]

        ids_in = sem("ids_in")
        ids_all_in = sem("ids_all_in")
        w_in = sem("w_in")
        clamped = sem("clamped")
        offsets_ready = sem("offsets_ready")
        mask_steps = sem("mask_steps")
        ident_steps = sem("ident_steps")
        ident_ready = sem("ident_ready")
        ident2_ready = sem("ident2_ready")
        ident4_ready = sem("ident4_ready")
        m_table_ready = sem("m_table_ready")
        a_raw_in = [sem(f"a_raw_in{k}") for k in range(A_RAWS)]
        b_raw_in = [sem(f"b_raw_in{k}") for k in range(2)]
        b_turned = sem("b_turned")
        b_moved = sem("b_moved")
        a_turned = sem("a_turned")
        a_lower = sem("a_lower")
        a_upper = sem("a_upper")
        x_in = [sem(f"x_in{k}") for k in range(UNROLL)]
        stored = [sem(f"stored{k}") for k in range(RING)]
        last_stored = sem("last_stored")
        xt_done = sem("xt_done")
        xt_moved = sem("xt_moved")
        b_staged = sem("b_staged")
        m_staged = sem("m_staged")
        slab_staged = sem("slab_staged")
        parts_done = sem("parts_done")
        parts_moved = sem("parts_moved")
        bx_done = sem("bx_done")
        spread_ready = sem("spread_ready")
        h_done = sem("h_done")
        h_moved = sem("h_moved")
        out_done = sem("out_done")
        out_moved = sem("out_moved")

        block = ctx.enter_context(nc.Block())

        def pairs(engine, step, first, last=0):
            turns = PAIRS // UNROLL
            for turn in range(first):
                for slot in range(UNROLL):
                    step(turn * UNROLL + slot, slot, turn)
            with engine.Fori(first, turns - last) as turn:
                for slot in range(UNROLL):
                    step(turn * UNROLL + slot, slot, turn)
            for turn in range(turns - last, turns):
                for slot in range(UNROLL):
                    step(turn * UNROLL + slot, slot, turn)

        def place(engine, kind, batch, last):
            return nc.values_load(
                offsets[:, kind, bass.ds(batch, 1)], engines=[engine], min_val=0, max_val=last,
                skip_runtime_bounds_check_because="the ids are clamped before the places are worked out",
            )

        @block.sync
        def _(sp):
            def load_b(n):
                k = n % 2
                wait(sp, b_turned, (n - 1) * 4)
                sp.dma_start(b_raw[:, k, :, :], b_loads[n]).then_inc(b_raw_in[k], 16)

            def load_a(g):
                k = g % A_RAWS
                wait(sp, a_turned, g - A_RAWS + 1)
                sp.dma_start(a_raw[:, k, :, :], a_loads[g]).then_inc(a_raw_in[k], 16)

            def load_x(pair, slot, turn):
                wait(sp, out_done, (pair - UNROLL + 1) * HALVES)
                sp.dma_start(moving[0:C, slot, 0, :], x_pairs[pair, 0]).then_inc(x_in[slot], 16)
                sp.dma_start(moving[C:P, slot, 1, :], x_pairs[pair, 1]).then_inc(x_in[slot], 16)

            def store(pair, slot, turn):
                sp.wait_ge(out_moved, (pair + 1) * HALVES)
                sp.dma_start(out_pairs[pair], result[:, slot % RING, :]).then_inc(stored[slot % RING], 16)

            for n, groups in enumerate(A_AFTER_B):
                load_b(n)
                for g in groups:
                    load_a(g)
            load_x(0, 0, 0)
            load_a(GROUPS - 1)
            for slot in range(1, RING):
                load_x(slot, slot, 0)
            sp.wait_ge(a_turned, GROUPS)
            sp.wait_ge(b_turned, 2 * GROUPS)
            for slot in range(RING, UNROLL):
                load_x(slot, slot, 0)
            with sp.Fori(1, PAIRS // UNROLL) as turn:
                for slot in range(UNROLL):
                    load_x(turn * UNROLL + slot, slot, turn)
                    store((turn - 1) * UNROLL + slot, slot, turn)
            for slot in range(UNROLL - 2):
                store(PAIRS - UNROLL + slot, slot, 0)
            for pair in range(PAIRS - 2, PAIRS):
                for half in range(HALVES):
                    sp.wait_ge(out_moved, pair * HALVES + half + 1)
                    cols = slice(half * BANK, (half + 1) * BANK)
                    sp.dma_start(out_pairs[pair][:, cols], result[:, pair % RING, cols]).then_inc(last_stored, 16)
            for k in range(RING):
                sp.wait_ge(stored[k], 16 * (PAIRS // RING - (k >= RING - 2)))
            sp.wait_ge(last_stored, 16 * 2 * HALVES)

        @block.gpsimd
        def _(pool):
            nc.gpsimd.memset(ident[:, :], 0.0).then_inc(ident_steps, 1)
            pool.wait_ge(ident_steps, 1)
            nc.gpsimd.affine_select(
                out=ident[:, :], in_=ident[:, :], compare_op=ALU.not_equal, fill=1.0, base=0,
                pattern=[[-1, P]], channel_multiplier=1,
            ).then_inc(ident_ready, 1)

            pool.wait_ge(ident2_ready, 1)
            pool.wait_ge(w_in, 16)
            for n, rows in enumerate((slice(C, P), slice(0, C))):
                wait(pool, m_table_ready, n)
                nc.gpsimd.tensor_tensor(
                    m_table[rows, :, :], m_table[0:C, :, :],
                    ident2[0:C, :].unsqueeze(1).to_broadcast([C, CONDS, C]), ALU.add,
                ).then_inc(m_table_ready, 1)

            pool.wait_ge(offsets_ready, 3)

            def stage(pair, slot, turn):
                at = [place(mybir.EngineType.Pool, B_AT, 2 * pair + h, (ADAPTERS - 1) * R) for h in range(2)]
                if isinstance(pair, int) and pair == 0:
                    pool.wait_ge(b_moved, 2 * GROUPS)
                wait(pool, parts_done, pair - RING + 1)
                for h in range(2):
                    nc.gpsimd.tensor_copy(
                        b_pair[:, slot % RING, :, h, :],
                        bt_table[:, :, :, :].rearrange("p j a r -> p j (a r)")[:, :, bass.ds(at[h], R)],
                    ).then_inc(b_staged, 1)

            pairs(pool, stage, first=1)

        @block.scalar
        def _(act):
            act.dma_start(ids[:, 0, :], cond_ids.rearrange("(o n) -> o n", o=1)).then_inc(ids_in, 16)
            act.dma_start(ids[:, 1, :], adapter_ids.rearrange("(o n) -> o n", o=1)).then_inc(ids_in, 16)
            act.dma_start(ids_all[:, :], adapter_ids.partition_broadcast(P)).then_inc(ids_all_in, 16)
            act.dma_start(m_table[0:C, :, :], cond_w.rearrange("w c d -> c w d")).then_inc(w_in, 16)

            def copy_upper(g):
                act.wait_ge(a_turned, g + 1)
                nc.scalar.copy(at_table[C:P, 2 * g + 1, :], at_table[0:C, 2 * g, :]).then_inc(a_upper, 1)

            def move_b(g, u):
                act.wait_ge(b_turned, 2 * g + u + 1)
                nc.scalar.copy(
                    bt_table[:, 4 * u : 4 * u + 4, g * PER_GROUP : (g + 1) * PER_GROUP, :].rearrange(
                        "p j a r -> p j (a r)"
                    ),
                    bank[(2 * g + u) % 8][:, :].rearrange("p (j c) -> p j c", c=P),
                ).then_inc(b_moved, 1)

            def move_x(pair, slot, half):
                act.wait_ge(xt_done, 2 * pair + half + 1)
                nc.scalar.copy(
                    x_t[:, slot % 2, :, half * C : half * C + C],
                    xt_bank[half][:, :].rearrange("p (j c) -> p j c", c=C),
                ).then_inc(xt_moved, 1)

            def move_out(pair, slot, half):
                act.wait_ge(out_done, HALVES * pair + half + 1)
                nc.scalar.copy(
                    result[:, slot % RING, half * BANK : (half + 1) * BANK], out_bank[2 * (slot % 2) + half][:, :]
                ).then_inc(out_moved, 1)

            def stage_m(pair, slot):
                m = m_table[:, :, :].rearrange("p w d -> p (w d)")
                at = [place(mybir.EngineType.Activation, M_AT, 2 * pair + h, (CONDS - 1) * C) for h in range(2)]
                wait(act, out_done, (pair - RING + 1) * HALVES)
                nc.scalar.copy(weights[0:C, slot % RING, 0, :], m[0:C, bass.ds(at[0], C)]).then_inc(m_staged, 1)
                nc.scalar.copy(weights[C:P, slot % RING, 1, :], m[C:P, bass.ds(at[1], C)]).then_inc(m_staged, 1)

            def move(pair, slot, turn):
                static = isinstance(pair, int)
                wait(act, stored[slot % RING], 16 * (turn * (UNROLL // RING) + slot // RING))
                move_out(pair, slot, 0)
                if not static or pair + 3 < PAIRS:
                    for half in range(2):
                        move_x(pair + 3, (slot + 3) % UNROLL, half)
                if not static or pair + 2 < PAIRS:
                    stage_m(pair + 2, (slot + 2) % UNROLL)
                move_out(pair, slot, 1)

            for n, groups in enumerate(A_AFTER_B):
                for g in (2 * n, 2 * n + 1):
                    for u in range(2):
                        move_b(g, u)
                for g in groups:
                    copy_upper(g)
            act.wait_ge(offsets_ready, 3)
            act.wait_ge(m_table_ready, 2)
            stage_m(0, 0)
            for half in range(2):
                move_x(0, 0, half)
            copy_upper(GROUPS - 1)
            for half in range(2):
                move_x(1, 1, half)
            stage_m(1, 1)
            for half in range(2):
                move_x(2, 2, half)
            pairs(act, move, first=1, last=1)

        @block.vector
        def _(dve):
            dve.wait_ge(ident_ready, 1)
            nc.vector.tensor_tensor(ident2[:, :], ident[:, 0:C], ident[:, C:P], ALU.add).then_inc(ident2_ready, 1)
            dve.wait_ge(ident2_ready, 1)
            nc.vector.tensor_tensor(
                ident4[:, :], ident2[:, 0 : 2 * R], ident2[:, 2 * R : 4 * R], ALU.add
            ).then_inc(ident4_ready, 1)

            def turn_a(g):
                dve.wait_ge(a_raw_in[g % A_RAWS], 16 * (g // A_RAWS + 1))
                nc.vector.transpose(
                    at_table[:, 2 * g, :].rearrange("p (w s) -> p s w", s=32),
                    a_raw[:, g % A_RAWS, :, :].rearrange("p e (s r) -> p s e r", r=R),
                ).then_inc(a_turned, 1)
                dve.wait_ge(a_turned, g + 1)
                nc.vector.tensor_copy(at_table[0:C, 2 * g + 1, :], at_table[C:P, 2 * g, :]).then_inc(a_lower, 1)

            turn_a(0)

            dve.wait_ge(ids_in, 32)
            adapter = ids[:, 1, :]
            nc.vector.tensor_scalar(cond_row[:, :], ids[:, 0, :], 0, CONDS - 1, ALU.max, ALU.min).then_inc(clamped, 1)
            nc.vector.tensor_scalar(adapter, adapter, 0, ADAPTERS - 1, ALU.max, ALU.min).then_inc(clamped, 1)
            dve.wait_ge(clamped, 2)
            nc.vector.tensor_scalar(offsets[:, M_AT, :], cond_row[:, :], C, None, ALU.mult).then_inc(offsets_ready, 1)
            nc.vector.tensor_scalar(offsets[:, B_AT, :], adapter, R, None, ALU.mult).then_inc(offsets_ready, 1)
            nc.vector.tensor_scalar(group_row[:, :], adapter, -PER_GROUP, None, ALU.bitwise_and).then_inc(clamped, 1)
            nc.vector.tensor_scalar(slab_row[:, :], adapter, 2, None, ALU.bitwise_and).then_inc(clamped, 1)
            dve.wait_ge(clamped, 4)
            of_even = slab_row[:, :].rearrange("o (n h) -> o h n", h=2)[:, 0]
            nc.vector.tensor_scalar(of_even, of_even, 2, None, ALU.bitwise_xor).then_inc(clamped, 1)
            nc.vector.tensor_scalar(group_row[:, :], group_row[:, :], 2 * T // PER_GROUP, None, ALU.mult).then_inc(
                clamped, 1
            )
            dve.wait_ge(clamped, 6)
            nc.vector.tensor_scalar(slab_row[:, :], slab_row[:, :], T // 2, None, ALU.mult).then_inc(clamped, 1)
            dve.wait_ge(clamped, 7)
            nc.vector.tensor_tensor(offsets[:, A_AT, :], group_row[:, :], slab_row[:, :], ALU.add).then_inc(
                offsets_ready, 1
            )

            turn_a(1)

            dve.wait_ge(ids_all_in, 16)
            nc.vector.tensor_scalar(ids_all[:, :], ids_all[:, :], 0, ADAPTERS - 1, ALU.max, ALU.min).then_inc(
                mask_steps, 1
            )
            dve.wait_ge(mask_steps, 1)
            nc.vector.tensor_scalar(in_slab[:, :], ids_all[:, :], 5, None, ALU.bitwise_and).then_inc(mask_steps, 1)
            dve.wait_ge(mask_steps, 2)
            own = in_slab[:, :].rearrange("p (n h) -> p h n", h=2)
            for h in range(2):
                rows = slice(h * C, h * C + C)
                for k, bits in enumerate((0, 4, 1, 5)):
                    nc.vector.tensor_scalar(slab_mask[rows, :, k], own[rows, h, :], bits, None, ALU.is_equal).then_inc(
                        mask_steps, 1
                    )
            dve.wait_ge(mask_steps, 2 + 2 * PER_SLAB)

            for g in range(2, GROUPS):
                turn_a(g)

            def slab_place(pair, h):
                return place(mybir.EngineType.DVE, A_AT, 2 * pair + h, (SLABS - 1) * T)

            def stage_slab(pair, slot, h, at):
                rows = slice(C, P) if h == 0 else slice(0, C)
                if isinstance(pair, int) and pair == 0:
                    dve.wait_ge(a_upper if h == 0 else a_lower, GROUPS)
                wait(dve, out_done, (pair - UNROLL + 1) * HALVES)
                nc.vector.tensor_copy(
                    moving[rows, slot, h, :], at_table[rows, :, :].rearrange("p s t -> p (s t)")[:, bass.ds(at, T)]
                ).then_inc(slab_staged, 1)

            def parts(pair):
                dve.wait_ge(parts_done, pair + 1)
                nc.vector.tensor_copy(bx_parts[:, :], parts_bank[:, 0:P]).then_inc(parts_moved, 1)

            def spread(pair):
                dve.wait_ge(bx_done, pair + 1)
                for h in range(2):
                    rows = slice(h * C, h * C + C)
                    nc.vector.tensor_tensor(
                        bx_spread[rows, :, :],
                        bx_cols[rows, :].unsqueeze(1).to_broadcast([C, PER_SLAB, R]),
                        slab_mask[rows, bass.ds(pair, 1), :].rearrange("p o k -> p (o k)").unsqueeze(2).to_broadcast(
                            [C, PER_SLAB, R]
                        ),
                        ALU.mult,
                    ).then_inc(spread_ready, 1)

            def move_h(pair, slot):
                dve.wait_ge(h_done, pair + 1)
                nc.vector.tensor_copy(weights[C:P, slot % RING, 0, :], h_cols[C:P, :]).then_inc(h_moved, 1)
                nc.vector.tensor_copy(weights[0:C, slot % RING, 1, :], h_cols[0:C, :]).then_inc(h_moved, 1)

            def step(pair, slot, turn):
                ahead = (slot + 1) % UNROLL
                static = isinstance(pair, int)
                if static and pair + 1 >= PAIRS:
                    return
                parts(pair + 1)
                if static and pair == 0:
                    at = [slab_place(1, h) for h in range(2)]
                    stage_slab(1, 1, 1, at[1])
                spread(pair + 1)
                if static and pair == 0:
                    stage_slab(1, 1, 0, at[0])
                more = not static or pair + 2 < PAIRS
                if more:
                    stage_slab(pair + 2, (slot + 2) % UNROLL, 0, slab_place(pair + 2, 0))
                move_h(pair + 1, ahead)
                if more:
                    stage_slab(pair + 2, (slot + 2) % UNROLL, 1, slab_place(pair + 2, 1))

            dve.wait_ge(offsets_ready, 3)
            at = [slab_place(0, h) for h in range(2)]
            parts(0)
            stage_slab(0, 0, 1, at[1])
            spread(0)
            stage_slab(0, 0, 0, at[0])
            move_h(0, 0)
            pairs(dve, step, first=1, last=1)

        @block.tensor
        def _(pe):
            pe.wait_ge(ident_ready, 1)

            def keep_busy(free_bank, products):
                for _ in range(products):
                    nc.tensor.transpose(free_bank[:, 0:P], ident[:, :], ident[:, :])

            for n, busy in enumerate(BUSY_BEFORE_B):
                banks = bank[4 * (n % 2) : 4 * (n % 2) + 4]
                wait(pe, b_moved, 4 * (n - 1))
                keep_busy(banks[0], busy)
                pe.wait_ge(b_raw_in[n % 2], 16 * (n // 2 + 1))
                for u in range(4):
                    for j in range(4):
                        done = nc.tensor.transpose(
                            banks[u][:, j * P : (j + 1) * P],
                            b_raw[:, n % 2, u // 2, (4 * (u % 2) + j) * P : (4 * (u % 2) + j + 1) * P],
                            ident[:, :],
                        )
                    done.then_inc(b_turned, 1)
            pe.wait_ge(b_moved, 2 * GROUPS - 4)
            keep_busy(bank[3], BUSY_BEFORE_PAIR[0])
            pe.wait_ge(b_moved, 2 * GROUPS)

            def arrived(slot, turn):
                pe.wait_ge(x_in[slot], 32 * (turn + 1))

            def transpose_x(slot, in_turns=True):
                pieces = [(j, half) for j in range(CHUNKS) for half in range(2)]
                if not in_turns:
                    pieces.sort(key=lambda piece: piece[1])
                for j, half in pieces:
                    rows = slice(half * C, half * C + C)
                    done = nc.tensor.transpose(
                        xt_bank[half][:, j * C : (j + 1) * C],
                        moving[rows, slot, half, j * P : (j + 1) * P],
                        ident[rows, rows],
                    )
                    if j == CHUNKS - 1:
                        done.then_inc(xt_done, 1)

            def project(pair, slot):
                pe.wait_ge(b_staged, 2 * (pair + 1))
                for j in range(CHUNKS):
                    q = j % QUADS
                    done = nc.tensor.matmul(
                        parts_bank[32 * q : 32 * q + 32, 0:P],
                        b_pair[:, slot % RING, j, :, :].rearrange("p h r -> p (h r)"),
                        x_t[:, slot % 2, j, :],
                        start=j < QUADS, stop=j >= QUADS,
                    )
                done.then_inc(parts_done, 1)

            def turn_parts():
                for h in range(2):
                    rows = slice(h * C, h * C + C)
                    done = nc.tensor.matmul(
                        bx_cols[rows, :], bx_parts[:, rows], ident4[:, h * R : h * R + R], start=True, stop=True
                    )
                done.then_inc(bx_done, 1)

            def apply_m(pair, slot):
                pe.wait_ge(m_table_ready, 2)
                pe.wait_ge(spread_ready, 2 * (pair + 1))
                pe.wait_ge(m_staged, 2 * (pair + 1))
                for h in range(2):
                    rows = slice(h * C, h * C + C)
                    to = slice(C, P) if h == 0 else slice(0, C)
                    done = nc.tensor.matmul(
                        h_cols[to, :],
                        bx_spread[rows, :, :].rearrange("p k r -> p (k r)"),
                        weights[rows, slot % RING, h, :],
                        start=True, stop=True,
                    )
                done.then_inc(h_done, 1)

            def multiply(pair, slot, half):
                if half == 0:
                    pe.wait_ge(slab_staged, 2 * (pair + 1))
                    pe.wait_ge(h_moved, 2 * (pair + 1))
                wait(pe, out_moved, 2 * (pair - 2) + half + 1)
                for h in range(2):
                    done = nc.tensor.matmul(
                        out_bank[2 * (slot % 2) + half][h * C : h * C + C, :],
                        weights[:, slot % RING, h, :],
                        moving[:, slot, h, half * BANK : (half + 1) * BANK],
                        start=True, stop=True,
                    )
                done.then_inc(out_done, 1)

            def step(pair, slot, turn):
                one = (slot + 1) % UNROLL
                three = (slot + 3) % UNROLL
                static = isinstance(pair, int)
                if not static or pair + 1 < PAIRS:
                    project(pair + 1, one)
                multiply(pair, slot, 0)
                if not static or pair + 1 < PAIRS:
                    pe.wait_ge(parts_moved, pair + 2)
                    if not static or pair + 3 < PAIRS:
                        arrived(three, turn + (slot + 3) // UNROLL)
                    if not static or pair + 2 < PAIRS:
                        pe.wait_ge(xt_moved, 2 * (pair + 3))
                    turn_parts()
                if not static or pair + 3 < PAIRS:
                    transpose_x(three)
                early = static and pair + 3 == PAIRS
                if early:
                    multiply(pair, slot, 1)
                if not static or pair + 1 < PAIRS:
                    apply_m(pair + 1, one)
                if not early:
                    multiply(pair, slot, 1)

            arrived(0, 0)
            transpose_x(0, in_turns=False)
            keep_busy(bank[3], BUSY_BEFORE_PAIR[1])
            pe.wait_ge(xt_moved, 2)
            project(0, 0)
            arrived(1, 0)
            transpose_x(1, in_turns=False)
            pe.wait_ge(ident4_ready, 1)
            pe.wait_ge(parts_moved, 1)
            turn_parts()
            keep_busy(bank[3], BUSY_BEFORE_PAIR[2])
            apply_m(0, 0)
            arrived(2, 0)
            pe.wait_ge(xt_moved, 4)
            transpose_x(2)
            pairs(pe, step, first=1, last=1)


_INS = ["x", "itok_B_0_15", "itok_B_4_50", "L0_cond_weights", "L1_cond_A", "L1_cond_B"]


def kernel(**inputs):
    import numpy as _np
    import concourse.bacc as _bacc
    from concourse import mybir as _mybir
    from concourse.bass_utils import run_bass_kernel_spmd as _run

    nc = _bacc.Bacc("TRN2", target_bir_lowering=False, num_devices=1)
    arrays, args = {}, []
    for name in _INS:
        a = _np.ascontiguousarray(inputs[name])
        arrays[f"in_{name}"] = a
        args.append(nc.dram_tensor(f"in_{name}", a.shape, _mybir.dt.from_np(a.dtype), kind="ExternalInput").ap())
    out = nc.dram_tensor("out_0", arrays["in_x"].shape, _mybir.dt.float32, kind="ExternalOutput").ap()
    cond_lora_kernel(nc, *args, out)
    r = _run(nc, [arrays], core_ids=[0])
    return r.results[0]["out_0"]
```
